# Optimizing a Trainium2 kernel written in Bass

```python
import numpy as np
import jax
import jax.numpy as jnp

def _softmax(x, axis=-1):
    return jax.nn.softmax(x, axis=axis)

def _gelu(x):
    return jax.nn.gelu(x, approximate=True)

def _silu(x):
    return jax.nn.silu(x)

def _sigmoid(x):
    return jax.nn.sigmoid(x)

def _layernorm(x, axis=-1, eps=1e-05):
    m = jnp.mean(x, axis=axis, keepdims=True)
    v = jnp.var(x, axis=axis, keepdims=True)
    return (x - m) / jnp.sqrt(v + eps)

def _scatter_add(tgt, idx, src, axis=0):
    return tgt.at[idx].add(src)

def _segment_sum(src, seg, n):
    return jax.ops.segment_sum(src, seg, n)
kernel_name = 'mk_gnn_resnorm_d4_gnn_r8_adf535'

def setup_inputs(seed: int=0):
    np.random.seed(seed)
    _w = jnp.asarray

    def _rec_inputs():
        import jax
        import jax.numpy as jnp
        _gk = jax.random.key(seed)
        x = -0.000202 + 1 * jax.random.normal(jax.random.fold_in(_gk, 1), (12500, 64), jnp.float32)
        src = jax.random.randint(jax.random.fold_in(_gk, 2), (400000,), 0, 12500, jnp.int32)
        dst = jnp.minimum((12500 * jax.random.uniform(jax.random.fold_in(_gk, 3), (400000,)) ** 2.0).astype(jnp.int32), 99999)
        _o = jnp.argsort(dst, stable=True)
        src = src[_o]
        dst = dst[_o]
        edge_attr_64 = 0.000189758 + 1.00013 * jax.random.normal(jax.random.fold_in(_gk, 13), (400000, 64), jnp.float32)
        edge_type_8 = jax.random.randint(jax.random.fold_in(_gk, 15), (400000,), 0, 8, jnp.int32)
        node_type_4 = jax.random.randint(jax.random.fold_in(_gk, 16), (12500,), 0, 4, jnp.int32)
        return (x, src, dst, edge_attr_64, edge_type_8, node_type_4)
    x, src, dst, edge_attr_64, edge_type_8, node_type_4 = _rec_inputs()

    def _L0_gnn_setup():
        import jax, jax.numpy as jnp
        import numpy as np
        N_NODES = 12500
        N_EDGES = 200000
        IN_CH = 64
        OUT_CH = 64
        key = jax.random.key(seed)
        ks = jax.random.split(key, 6)
        x = jax.random.normal(ks[0], (N_NODES, IN_CH), dtype=jnp.float32)
        edge_index = jax.random.randint(ks[1], (2, N_EDGES), 0, N_NODES, dtype=jnp.int64)
        W1 = jax.random.normal(ks[2], (2 * IN_CH, OUT_CH), dtype=jnp.float32) * (1.0 / np.sqrt(2 * IN_CH))
        b1 = jnp.zeros((OUT_CH,), dtype=jnp.float32)
        W2 = jax.random.normal(ks[3], (OUT_CH, OUT_CH), dtype=jnp.float32) * (1.0 / np.sqrt(OUT_CH))
        b2 = jnp.zeros((OUT_CH,), dtype=jnp.float32)
        return {'x': x, 'edge_index': edge_index, 'W1': W1, 'b1': b1, 'W2': W2, 'b2': b2}
    _L0_gnn_all = _L0_gnn_setup()
    _L0_gnn_in = {k: v for k, v in _L0_gnn_all.items() if k in ('W1', 'b1', 'W2', 'b2')}
    del _L0_gnn_all

    def _L1_gnn_setup():
        import jax, jax.numpy as jnp
        import numpy as np
        N_NODES = 6250
        N_EDGES = 100000
        N_GRAPHS = 128
        D = 64
        key = jax.random.key(seed)
        ks = jax.random.split(key, 8)
        x = jax.random.normal(ks[0], (N_NODES, D), dtype=jnp.float32)
        edge_index = jax.random.randint(ks[1], (2, N_EDGES), 0, N_NODES, dtype=jnp.int64)
        edge_attr = jax.random.normal(ks[2], (N_EDGES, D), dtype=jnp.float32)
        u = jax.random.normal(ks[3], (N_GRAPHS, D), dtype=jnp.float32)
        batch = jnp.sort(jax.random.randint(ks[4], (N_NODES,), 0, N_GRAPHS, dtype=jnp.int64))
        W1 = jax.random.normal(ks[5], (3 * D, D), dtype=jnp.float32) * (1.0 / np.sqrt(3 * D))
        b1 = jnp.zeros((D,), dtype=jnp.float32)
        W2 = jax.random.normal(ks[6], (D, D), dtype=jnp.float32) * (1.0 / np.sqrt(D))
        b2 = jnp.zeros((D,), dtype=jnp.float32)
        return {'x': x, 'edge_index': edge_index, 'edge_attr': edge_attr, 'u': u, 'batch': batch, 'W1': W1, 'b1': b1, 'W2': W2, 'b2': b2}
    _L1_gnn_all = _L1_gnn_setup()
    _L1_gnn_in = {k: v for k, v in _L1_gnn_all.items() if k in ('u', 'W1', 'b1', 'W2', 'b2')}
    del _L1_gnn_all

    def _L2_gnn_setup():
        import jax, jax.numpy as jnp
        import numpy as np
        N_NODES = 12500
        N_EDGES = 125000
        D_IN = 64
        D_OUT = 64
        GROUPS = 3
        key = jax.random.key(seed)
        ks = jax.random.split(key, 7)
        feature = jax.random.normal(ks[0], (N_NODES, D_IN), dtype=jnp.float32)
        src = jax.random.randint(ks[1], (N_EDGES,), 0, N_NODES)
        dst = jax.random.randint(ks[2], (N_EDGES,), 0, N_NODES)
        W_gc = jax.random.normal(ks[3], (D_IN, GROUPS), dtype=jnp.float32)
        b_gc = jax.random.normal(ks[4], (1, GROUPS), dtype=jnp.float32)
        W_lin = jax.random.normal(ks[5], (D_OUT, D_IN), dtype=jnp.float32) * (1.0 / np.sqrt(D_IN))
        b_lin = jax.random.normal(ks[6], (D_OUT,), dtype=jnp.float32) * 0.01
        return {'feature': feature, 'src': src, 'dst': dst, 'W_gc': W_gc, 'b_gc': b_gc, 'W_lin': W_lin, 'b_lin': b_lin}
    _L2_gnn_all = _L2_gnn_setup()
    _L2_gnn_in = {k: v for k, v in _L2_gnn_all.items() if k in ('W_gc', 'b_gc', 'W_lin', 'b_lin')}
    del _L2_gnn_all

    def _L3_gnn_setup():
        import jax, jax.numpy as jnp
        import numpy as np
        N, E = (5000, 80000)
        IN, H, HS = (64, 4, 16)
        NT, ET = (4, 8)

        def typed_linear(x, W, types):
            out = jnp.zeros((x.shape[0], W.shape[-1]), x.dtype)
            for t in range(W.shape[0]):
                out = out + jnp.where((types == t)[:, None], x @ W[t], 0.0)
            return out

        def typed_head_linear(z, W, types):
            out = jnp.zeros_like(z)
            for t in range(W.shape[1]):
                out = out + jnp.where((types == t)[:, None, None], jnp.einsum('ehd,hdo->eho', z, W[:, t]), 0.0)
            return out
        key = jax.random.key(seed)
        ks = jax.random.split(key, 12)
        x = jax.random.normal(ks[0], (N, IN), jnp.float32)
        ntype = jax.random.randint(ks[1], (N,), 0, NT)
        etype = jax.random.randint(ks[2], (E,), 0, ET)
        src = jax.random.randint(ks[3], (E,), 0, N)
        dst = jax.random.randint(ks[4], (E,), 0, N)
        s_in = 1.0 / np.sqrt(IN).astype(np.float32)
        s_hs = 1.0 / np.sqrt(HS).astype(np.float32)
        s_m = 1.0 / np.sqrt(H * HS).astype(np.float32)
        Wk = jax.random.normal(ks[5], (NT, IN, H * HS), jnp.float32) * s_in
        Wq = jax.random.normal(ks[6], (NT, IN, H * HS), jnp.float32) * s_in
        Wv = jax.random.normal(ks[7], (NT, IN, H * HS), jnp.float32) * s_in
        Wa = jax.random.normal(ks[8], (NT, H * HS, H * HS), jnp.float32) * s_m
        rel_att = jax.random.normal(ks[9], (H, ET, HS, HS), jnp.float32) * s_hs
        rel_msg = jax.random.normal(ks[10], (H, ET, HS, HS), jnp.float32) * s_hs
        rel_pri = jnp.ones((H, ET), jnp.float32)
        return {'x': x, 'ntype': ntype, 'etype': etype, 'src': src, 'dst': dst, 'Wk': Wk, 'Wq': Wq, 'Wv': Wv, 'Wa': Wa, 'rel_att': rel_att, 'rel_msg': rel_msg, 'rel_pri': rel_pri}
    _L3_gnn_all = _L3_gnn_setup()
    _L3_gnn_in = {k: v for k, v in _L3_gnn_all.items() if k in ('Wk', 'Wq', 'Wv', 'Wa', 'rel_att', 'rel_msg', 'rel_pri')}
    del _L3_gnn_all
    return {'x': x, 'src': src, 'dst': dst, 'edge_attr_64': edge_attr_64, 'edge_type_8': edge_type_8, 'node_type_4': node_type_4, 'L0_gnn_W1': _L0_gnn_in['W1'], 'L0_gnn_b1': _L0_gnn_in['b1'], 'L0_gnn_W2': _L0_gnn_in['W2'], 'L0_gnn_b2': _L0_gnn_in['b2'], 'L1_gnn_u': _L1_gnn_in['u'], 'L1_gnn_W1': _L1_gnn_in['W1'], 'L1_gnn_b1': _L1_gnn_in['b1'], 'L1_gnn_W2': _L1_gnn_in['W2'], 'L1_gnn_b2': _L1_gnn_in['b2'], 'L2_gnn_W_gc': _L2_gnn_in['W_gc'], 'L2_gnn_b_gc': _L2_gnn_in['b_gc'], 'L2_gnn_W_lin': _L2_gnn_in['W_lin'], 'L2_gnn_b_lin': _L2_gnn_in['b_lin'], 'L3_gnn_Wk': _L3_gnn_in['Wk'], 'L3_gnn_Wq': _L3_gnn_in['Wq'], 'L3_gnn_Wv': _L3_gnn_in['Wv'], 'L3_gnn_Wa': _L3_gnn_in['Wa'], 'L3_gnn_rel_att': _L3_gnn_in['rel_att'], 'L3_gnn_rel_msg': _L3_gnn_in['rel_msg'], 'L3_gnn_rel_pri': _L3_gnn_in['rel_pri']}

def reference(x, src, dst, edge_attr_64, edge_type_8, node_type_4, L0_gnn_W1, L0_gnn_b1, L0_gnn_W2, L0_gnn_b2, L1_gnn_u, L1_gnn_W1, L1_gnn_b1, L1_gnn_W2, L1_gnn_b2, L2_gnn_W_gc, L2_gnn_b_gc, L2_gnn_W_lin, L2_gnn_b_lin, L3_gnn_Wk, L3_gnn_Wq, L3_gnn_Wv, L3_gnn_Wa, L3_gnn_rel_att, L3_gnn_rel_msg, L3_gnn_rel_pri):
    import jax
    import jax.numpy as jnp

    def _L0_gnn_ref(x, edge_index, W1, b1, W2, b2):
        import jax, jax.numpy as jnp
        import numpy as np
        N_NODES = 12500
        N_EDGES = 200000
        IN_CH = 64
        OUT_CH = 64
        src = edge_index[0]
        dst = edge_index[1]
        x_i = x[dst]
        x_j = x[src]
        edge_features = jnp.concatenate([x_i, x_j - x_i], axis=-1)
        h = jax.nn.relu(edge_features @ W1 + b1)
        edge_messages = h @ W2 + b2
        out = jax.ops.segment_max(edge_messages, dst, num_segments=x.shape[0])
        return jnp.where(jnp.isfinite(out), out, jnp.zeros_like(out))

    def _L1_gnn_ref(x, edge_index, edge_attr, u, batch, W1, b1, W2, b2):
        import jax, jax.numpy as jnp
        import numpy as np
        N_NODES = 6250
        N_EDGES = 100000
        N_GRAPHS = 128
        D = 64
        n_nodes = x.shape[0]
        src = edge_index[0]
        sums = jax.ops.segment_sum(edge_attr, src, num_segments=n_nodes)
        cnt = jax.ops.segment_sum(jnp.ones((edge_attr.shape[0],), edge_attr.dtype), src, num_segments=n_nodes)
        v_e = sums / jnp.maximum(cnt, 1.0)[:, None]
        comb = jnp.concatenate([x, v_e, u[batch]], axis=1)
        h = jax.nn.relu(comb @ W1 + b1)
        out = jax.nn.relu(h @ W2 + b2)
        return out

    def _L2_gnn_ref(feature, src, dst, W_gc, b_gc, W_lin, b_lin):
        import jax, jax.numpy as jnp
        import numpy as np
        N_NODES = 12500
        N_EDGES = 125000
        D_IN = 64
        D_OUT = 64
        GROUPS = 3
        N = feature.shape[0]
        msg_sum = jax.ops.segment_sum(feature[src], dst, num_segments=N)
        deg = jax.ops.segment_sum(jnp.ones_like(src, dtype=feature.dtype), dst, num_segments=N)
        h = jnp.where(deg[:, None] > 0, msg_sum / jnp.maximum(deg, 1.0)[:, None], 0.0)
        ge = jax.nn.relu(h @ W_gc + b_gc)
        top = jnp.max(ge, axis=-1, keepdims=True)
        mask = (ge == top).astype(h.dtype)
        h = h * jnp.sum(mask, axis=-1, keepdims=True)
        return h @ W_lin.T + b_lin

    def _L3_gnn_ref(x, ntype, etype, src, dst, Wk, Wq, Wv, Wa, rel_att, rel_msg, rel_pri):
        import jax, jax.numpy as jnp
        import numpy as np
        N, E = (5000, 80000)
        IN, H, HS = (64, 4, 16)
        NT, ET = (4, 8)

        def typed_linear(x, W, types):
            out = jnp.zeros((x.shape[0], W.shape[-1]), x.dtype)
            for t in range(W.shape[0]):
                out = out + jnp.where((types == t)[:, None], x @ W[t], 0.0)
            return out

        def typed_head_linear(z, W, types):
            out = jnp.zeros_like(z)
            for t in range(W.shape[1]):
                out = out + jnp.where((types == t)[:, None, None], jnp.einsum('ehd,hdo->eho', z, W[:, t]), 0.0)
            return out
        n = x.shape[0]
        h_heads, hs = (rel_att.shape[0], rel_att.shape[-1])
        sqrt_d = jnp.asarray(np.sqrt(hs), x.dtype)
        k = typed_linear(x, Wk, ntype).reshape(n, h_heads, hs)
        q = typed_linear(x, Wq, ntype).reshape(n, h_heads, hs)
        v = typed_linear(x, Wv, ntype).reshape(n, h_heads, hs)
        ke, qe, ve = (k[src], q[dst], v[src])
        kw = typed_head_linear(ke, rel_att, etype)
        qw = typed_head_linear(qe, rel_att, etype)
        a = (kw * qw).sum(-1) * rel_pri[:, etype].T / sqrt_d
        m = typed_head_linear(ve, rel_msg, etype)
        amax = jax.ops.segment_max(a, dst, num_segments=n)
        ex = jnp.exp(a - amax[dst])
        denom = jax.ops.segment_sum(ex, dst, num_segments=n)
        alpha = ex / denom[dst]
        h = jax.ops.segment_sum(m * alpha[:, :, None], dst, num_segments=n)
        h = h.reshape(n, h_heads * hs)
        return typed_linear(h, Wa, ntype)
    edge_index = jnp.stack([src, dst])
    batch0 = jnp.zeros((12500,), jnp.int32)
    x = _layernorm(x + _L0_gnn_ref(x, edge_index, L0_gnn_W1, L0_gnn_b1, L0_gnn_W2, L0_gnn_b2), axis=-1)
    x = _layernorm(x + _L1_gnn_ref(x, edge_index, edge_attr_64, L1_gnn_u, batch0, L1_gnn_W1, L1_gnn_b1, L1_gnn_W2, L1_gnn_b2), axis=-1)
    x = _layernorm(x + _L2_gnn_ref(x, src, dst, L2_gnn_W_gc, L2_gnn_b_gc, L2_gnn_W_lin, L2_gnn_b_lin), axis=-1)
    x = _layernorm(x + _L3_gnn_ref(x, node_type_4, edge_type_8, src, dst, L3_gnn_Wk, L3_gnn_Wq, L3_gnn_Wv, L3_gnn_Wa, L3_gnn_rel_att, L3_gnn_rel_msg, L3_gnn_rel_pri), axis=-1)
    return x

_drawn_inputs = setup_inputs


def setup_inputs(seed=0):
    import zlib

    import numpy as np

    out = dict(_drawn_inputs(seed))
    spreads = {'L0_gnn_b1': (0.0, 0.1),
     'L0_gnn_b2': (0.0, 0.1),
     'L1_gnn_b1': (0.0, 0.1),
     'L1_gnn_b2': (0.0, 0.1),
     'L3_gnn_rel_pri': (1.0, 0.2)}
    factors = {'L2_gnn_W_gc': 8.0, 'L2_gnn_b_lin': 4.533}
    for name, (base, spread) in spreads.items():
        noise = np.random.default_rng([zlib.crc32(name.encode()), seed]).standard_normal(out[name].shape)
        drawn = base * np.exp(spread * noise) if base else spread * noise
        out[name] = jnp.asarray(drawn.astype(out[name].dtype))
    for name, factor in factors.items():
        out[name] = (out[name] * factor).astype(out[name].dtype)
    return out
```

```python
from contextlib import ExitStack

import concourse.bass as bass
from concourse import mybir


P = 128
SUB = 5
KS = 5
COLS = SUB * KS
F = 64
NB = 7
H, HD, ET, NTY = 4, 16, 8, 4
HR = HD + 1
ROW3 = H * (HR + 1)
AGW = F + 1
LN_EPS = 1e-5
FAR = 1.0e30
SKIP = 1.0e6

F32 = mybir.dt.float32
BF16 = mybir.dt.bfloat16
I32 = mybir.dt.int32
U8 = mybir.dt.uint8
ALU = mybir.AluOpType
ACT = mybir.ActivationFunctionType
AX = mybir.AxisListType.X


def spread(ap, n):
    return ap.unsqueeze(len(ap.shape)).broadcast_to([*ap.shape, n])


def spread_mid(ap, n):
    return ap.unsqueeze(1).broadcast_to([ap.shape[0], n, ap.shape[1]])


def rows(table, index):
    return bass.IndirectOffsetOnAxis(ap=index, axis=0)


class Link:

    def __init__(self, eng, sem, base):
        self.eng, self.sem, self.base, self.n = eng, sem, base, 0

    def __call__(self, ins):
        ins.then_inc(self.sem, 1)
        self.n += 1
        self.eng.wait_ge(self.sem, self.base + self.n)


def gnn_program(nc, x, src, dst, attr, etype, ntype, w, out):
    N, E = x.shape[0], src.shape[0]
    J = E // P
    CL = J // SUB
    T = J // COLS
    NG = T * KS
    NC = P * SUB
    NT = -(-N // P)
    NP = NT * P
    NBAT = NT // NB
    LAST = N - (NT - 1) * P
    assert E == P * SUB * CL and T * KS == CL and T % 2 == 1 and NT % NB == 0 and NBAT % 2 == 0 and NBAT >= 4
    AGR = NP + P

    def scratch(name, shape, dt=F32):
        return nc.dram_tensor(name, shape, dt, kind="Internal").ap()

    starts_d = scratch("start_rows", (E, F))
    agg_d = [scratch(f"agg{r}", (AGR, AGW)) for r in range(SUB)]
    tab_a = scratch("tab_a", (NP, F))
    tab_b = scratch("tab_b", (NP, F))
    run0 = scratch("run0", (E, F))
    car0 = scratch("car0", (NC + 1, F))
    tab_x2 = scratch("tab_x2", (NP, F))
    run2 = scratch("run2", (E, F))
    car2 = scratch("car2", (NC + 1, F))
    tab_q = scratch("tab_q", (NP, F))
    tab_t = scratch("tab_t", (NP * ET, 2 * F))
    run3 = scratch("run3", (E, ROW3))
    car3 = scratch("car3", (NC + 1, ROW3))

    def chains(d):
        return d.rearrange("(p s i) f -> p s (i f)", p=P, s=SUB)

    def node_tiles(d):
        return d.rearrange("(t p) f -> p t f", p=P)

    with ExitStack() as ctx, ExitStack() as ctx_a, ExitStack() as ctx_e, ExitStack() as ctx_l:
        def sb(name, shape, dt=F32, stack=ctx):
            return stack.enter_context(nc.sbuf_tensor(name, shape, dt))

        def sem(name):
            return ctx.enter_context(nc.semaphore(name))

        pair = [ctx.enter_context(nc.psum_tensor(f"pair{i}", [P, 1024], F32)) for i in range(2)]
        bank = [ctx.enter_context(nc.psum_tensor(f"bank{i}", [P, 512], F32)) for i in range(4)]

        x_sb = sb("x_sb", [P, NT + NB, F])
        side = sb("side", [P, NT, F])
        src_i = sb("src_i", [P, SUB, CL + KS], I32)
        t_idx = sb("t_idx", [P, SUB, CL + KS], I32)
        cont = sb("cont", [P, SUB, CL + KS])
        first_i = sb("first_i", [P, SUB], I32)
        ident = sb("ident", [P, P])
        upper = sb("upper", [P, P])
        ones = sb("ones", [P, P])
        idn_bf = sb("idn_bf", [P, P], BF16)
        ones_bf = sb("ones_bf", [P, 2], BF16)
        zero_bf = sb("zero_bf", [P, P], BF16)
        iota_i = sb("iota_i", [P, P], I32)
        iota_bf = sb("iota_bf", [P, P], BF16)
        spare_i = sb("spare_i", [P, 1], I32)
        spare = sb("spare", [P, 1])
        marks = sb("marks", [P, 20])
        eps_c = sb("eps_c", [P, 1])
        far_c = sb("far_c", [P, 1])
        deg = sb("deg", [P, NT])
        dmask = sb("dmask", [P, NT])
        rdeg = sb("rdeg", [P, NT])
        start_x = sb("start_x", [P, NT], I32)
        end_x = sb("end_x", [P, NT + 2 * NB], I32)
        car_x = sb("car_x", [P, NT + 2 * NB], I32)
        joins_i = sb("joins_i", [1, 2, NC], I32)
        joins = sb("joins", [1, 2, NC])
        fj = sb("fj", [P, NC])
        fjp = sb("fjp", [P, NC])
        nt_i = sb("nt_i", [P, NT], I32)
        nmask = sb("nmask", [P, NTY, NT + 1])
        w_ab = sb("w_ab", [F, 2, F])
        b1_0 = sb("b1_0", [P, F])
        b2_0 = sb("b2_0", [P, F])
        w2_0 = sb("w2_0", [P, 2, F])
        w1_1 = sb("w1_1", [P, F])
        w1u_1 = sb("w1u_1", [F, F])
        u_col = sb("u_col", [F, 1])
        b1_1 = sb("b1_1", [F, 1])
        c_1 = sb("c_1", [F, 1])
        w2_1 = sb("w2_1", [F, F])
        b2_1 = sb("b2_1", [P, F])
        w_2 = sb("w_2", [F, F + 3])
        bgc = sb("bgc", [P, 3])
        blin = sb("blin", [P, F])
        w_kvq = sb("w_kvq", [P, NTY // 2, 3 * F])
        w_a3 = sb("w_a3", [F, NTY, F])
        rat = sb("rat", [F, ET, F])
        w_rel = sb("w_rel", [P, ET, 2 * F])
        pri = sb("pri", [F, H, ET])

        A = ctx_a
        dst_i = sb("dst_i", [P, SUB, CL], I32, A)
        part_i = sb("part_i", [P, SUB, CL], I32, A)
        s_hi = sb("s_hi", [P, SUB, CL + KS], U8, A)
        s_lo = sb("s_lo", [P, SUB, CL + KS], U8, A)
        d_hi = sb("d_hi", [P, SUB, CL + KS], U8, A)
        d_lo = sb("d_lo", [P, SUB, CL + KS], U8, A)
        zeros = sb("zeros", [P, COLS * F], F32, A)
        at = [sb(f"at{i}", [P, SUB, KS, F], F32, A) for i in range(2)]
        st_hi = [sb(f"st_hi{i}", [P, SUB, KS], BF16, A) for i in range(2)]
        st_lo = [sb(f"st_lo{i}", [P, SUB, KS], BF16, A) for i in range(2)]
        st_dh = [sb(f"st_dh{i}", [P, SUB, KS], BF16, A) for i in range(2)]
        st_dl = [sb(f"st_dl{i}", [P, SUB, KS], BF16, A) for i in range(2)]
        st_s = [sb(f"st_s{i}", [P, SUB, KS], F32, A) for i in range(2)]
        st_d = [sb(f"st_d{i}", [P, SUB, KS], F32, A) for i in range(2)]
        L = ctx_l
        xst = sb("xst", [P, NB, F], F32, L)
        bst = [sb(f"bst{i}", [P, NB, F], F32, L) for i in range(2)]
        xTs = [sb(f"xTs{i}", [F, NB, P], F32, L) for i in range(2)]
        L.close()
        same = [sb(f"same{i}", [P, SUB, P], F32, A) for i in range(2)]
        same_bf = [sb(f"same_bf{i}", [P, SUB, P], BF16, A) for i in range(2)]
        before = [sb(f"before{i}", [P, SUB, P], BF16, A) for i in range(2)]
        oh_lo = [sb(f"oh_lo{i}", [P, SUB, P], BF16, A) for i in range(2)]
        oh_hi = [sb(f"oh_hi{i}", [P, SUB, NT], BF16, A) for i in range(2)]
        sums = sb("sums", [P, KS, SUB, AGW], F32, A)
        ag_t = sb("ag_t", [P, SUB], F32, A)
        ag_idx = sb("ag_idx", [P, KS, SUB], I32, A)
        nwork = sb("nwork", [P, 8, NT], F32, A)
        nwork_i = sb("nwork_i", [P, NT], I32, A)
        A.close()

        gi = [sb(f"gi{i}", [P, SUB, KS], I32) for i in range(2)]
        ct = [sb(f"ct{i}", [P, SUB, KS]) for i in range(2)]
        pn = [sb(f"pn{i}", [P, SUB, KS]) for i in range(2)]
        cur = sb("cur", [P, SUB, F])
        zst = sb("zst", [P, SUB, ROW3])
        ar = sb("ar", [P, SUB, H])
        mp = sb("mp", [P, SUB, H])
        dm = [sb(f"dm{i}", [P, 2, SUB, H]) for i in range(2)]
        al = [sb(f"al{i}", [P, SUB, H]) for i in range(2)]
        first_rows = sb("first_rows", [P, SUB, F])
        tails = sb("tails", [P, SUB, 2, H * HR])
        tailT = sb("tailT", [P, 2, NC])
        fullT = sb("fullT", [P, 4, NC])
        full = sb("full", [P, SUB, ROW3])
        neutral = sb("neutral", [1, ROW3])
        est = [sb(f"est{i}", [P, NB], I32) for i in range(2)]
        cst = [sb(f"cst{i}", [P, NB], I32) for i in range(2)]
        sm = sb("sm", [P, 8, NB])
        s4 = sb("s4", [P, 6, NB, H])

        EDG = ctx_e
        gat = sb("gat", [P, KS, SUB, 2 * F], F32, EDG)
        edge0 = [sb(f"edge0{i}", [P, SUB, KS, F], F32, EDG) for i in range(2)]
        run_sb = [sb(f"run_sb{i}", [P, SUB, KS * ROW3], F32, EDG) for i in range(2)]
        t1 = sb("t1", [P, SUB, F], F32, EDG)
        p1 = sb("p1", [P, SUB, F], F32, EDG)
        ub = [sb(f"ub{i}", [P, SUB, F], F32, EDG) for i in range(2)]
        hT = [sb(f"hT{i}", [P, 3, P], F32, EDG) for i in range(2)]
        pr = sb("pr", [P, SUB, F], F32, EDG)
        wm = [sb(f"wm{i}", [P, SUB, H, HR], F32, EDG) for i in range(2)]
        ta = sb("ta", [P, SUB, H, HR], F32, EDG)
        EDG.close()

        r1 = [sb(f"r1{i}", [P, NB, ROW3]) for i in range(2)]
        r2 = [sb(f"r2{i}", [P, NB, ROW3]) for i in range(2)]
        ac = [sb(f"ac{i}", [P, SUB, NB, AGW]) for i in range(2)]
        comb = sb("comb", [P, NB, 2 * F])
        yb = sb("yb", [P, NB, F])
        zb = sb("zb", [P, NB, F])
        sq = sb("sq", [P, NB, F])
        cT = sb("cT", [P, NB, P])
        hTn = sb("hTn", [F, NB, P])
        xm = [sb(f"xm{i}", [P, NTY, F]) for i in range(2)]
        xmT = [sb(f"xmT{i}", [P, NTY // 2, P]) for i in range(2)]
        kvT = [sb(f"kvT{i}", [P, P]) for i in range(2)]
        trow = [sb(f"trow{i}", [P, ET, 2 * F]) for i in range(2)]
        sel = sb("sel", [P, NB, F])

        ids_in, w_in, x_in, oob_in = sem("ids_in"), sem("w_in"), sem("x_in"), sem("joins_in")
        pre, prep_m, wprep2, a_tt = sem("pre"), sem("prep_m"), sem("wprep2"), sem("a_term")
        a_sb = sem("a_same_bf")
        cst_p, cst_v, zeroed, prep, wprep = sem("cst_p"), sem("cst_v"), sem("zeroed"), sem("prep"), sem("wprep")
        e0_z, agg_z = sem("starts_zeroed"), sem("agg_zeroed")
        l_st, l_tr, l_ev, l_mm, l_a, l_b, l_ao = [sem("l_" + n) for n in
                                                 ("staged", "tr", "ev", "mm", "a", "b", "a_out")]
        l_out = [sem(f"l_b_out{i}") for i in range(2)]
        a_st, a_bc, a_eq, a_su, a_oh, a_red, a_row, a_idx, a_hist, a_pre, a_done = [
            sem("a_" + n) for n in ("staged", "bcast", "same", "before", "onehot", "reduced", "rowsum",
                                    "index", "hist", "prefix", "indices")]
        a_ld = [sem(f"a_ld{i}") for i in range(2)]
        a_sc = [sem(f"a_scat{i}") for i in range(SUB)]
        fr, fr_w, scat = sem("first_rows_in"), sem("first_rows_out"), sem("starts_scattered")
        b_t1, b_p1, b_a, b_s, b_u, b_tr, b_h, b_msg, b_st = [
            sem("b_" + n) for n in ("keep", "open", "side", "run", "sum", "tr", "relu", "msg", "staged")]
        c_t1, c_s, c_st = sem("c_keep"), sem("c_run"), sem("c_staged")
        d_t1, d_q, d_pr, d_ar, d_mp, d_m, d_dm, d_ex, d_wm, d_ta, d_acc, d_st = [
            sem("d_" + n) for n in ("keep", "side", "prod", "score", "open", "max", "diff", "exp", "wmsg",
                                    "decay", "acc", "staged")]
        g_in = {c: [sem(f"{c}_gat{i}") for i in range(KS)] for c in "bcd"}
        e_in = {c: [sem(f"{c}_side_in{i}") for i in range(2)] for c in "bd"}
        r_out = {c: [sem(f"{c}_run_out{i}") for i in range(2)] for c in "bcd"}
        k_tl, k_tr, k_ev, k_fu, k_tb, k_row, k_out, k_sc = [
            sem("k_" + n) for n in ("tails", "tr", "ev", "full", "trback", "rows", "out", "scan")]
        n_st = {c: sem(f"n{c}_staged") for c in "123"}
        n_r = {c: [sem(f"n{c}_rows{i}") for i in range(2)] for c in "123"}
        n_ac = [sem(f"n_agg{i}") for i in range(2)]
        n_use = {c: sem(f"n{c}_used") for c in "123"}
        n_v, n_s, n_m, n_a2 = [{c: sem(f"n{c}_{n}") for c in "123"} for n in ("dve", "sqrt", "pe", "act")]
        n_out = {c: sem(f"n{c}_out") for c in "12"}
        tp1, tp2, tp4, tq = sem("t_xT"), sem("t_proj"), sem("t_prod"), sem("t_queries")
        ta1, ta2, ta3, tv = sem("t_xT_sb"), sem("t_kvT_sb"), sem("t_rows"), sem("t_masked")
        t_o = [sem(f"t_out{i}") for i in range(2)]
        ch_pre, ch_k = sem("ch_pre"), sem("ch_k")
        ch_n = {c: sem(f"ch_n{c}") for c in "123"}
        o_out = sem("out_written")

        def run_view(tp, width):
            return run_sb[tp][:, :, 0:KS * width].rearrange("p s (k f) -> p s k f", f=width)

        ZR = 9
        AFL = AGR // P * AGW
        AGG_Z = 16 * SUB * -(-AFL // (COLS * F))

        def sides(t, tp):
            return t * 8 + (16 if tp == 0 else 8)

        def loop(eng, *bounds):
            return nc.Fori(*bounds, engines=(eng.engine,), hint_back_edge=True)

        def each_iteration(eng, body):
            body(0, 0, True)
            with loop(eng, 1, T - 1, 2) as t:
                body(t, 1, False)
                body(t + 1, 0, False)

        wide = lambda v: v.rearrange("(a n) -> a n", a=1).partition_broadcast(P).rearrange("p a n -> p (a n)")
        col = lambda v: v.rearrange("(n a) -> n a", a=1)
        W1, W2 = w["L0_gnn_W1"], w["L0_gnn_W2"]
        loads = [
            (w_ab[:, 0, :], W1[0:F, :]), (w_ab[:, 1, :], W1[F:2 * F, :]),
            (w2_0[0:F, 0, :], W2), (w2_0[F:P, 1, :], W2),
            (b1_0[:], wide(w["L0_gnn_b1"])), (b2_0[:], wide(w["L0_gnn_b2"])),
            (w1_1[:], w["L1_gnn_W1"][0:2 * F, :]), (w1u_1[:], w["L1_gnn_W1"][2 * F:3 * F, :]),
            (u_col[:], col(w["L1_gnn_u"][0])), (b1_1[:], col(w["L1_gnn_b1"])),
            (w2_1[:], w["L1_gnn_W2"]), (b2_1[:], wide(w["L1_gnn_b2"])),
            (w_2[:, 0:F], w["L2_W_lin_T"]), (w_2[:, F:F + 3], w["L2_gnn_W_gc"]),
            (bgc[:], wide(w["L2_gnn_b_gc"][0])), (blin[:], wide(w["L2_gnn_b_lin"])),
        ]
        for ty in range(NTY):
            for i, n in enumerate(("k", "v", "q")):
                loads.append((w_kvq[ty % 2 * F:ty % 2 * F + F, ty // 2, i * F:(i + 1) * F], w[f"L3_gnn_W{n}"][ty]))
            loads.append((w_a3[:, ty, :], w["L3_gnn_Wa"][ty]))
        for h in range(H):
            hs = slice(h * HD, (h + 1) * HD)
            loads.append((rat[hs, :, hs], w["L3_rel_att_T"][h]))
            loads.append((w_rel[F + h * HD:F + (h + 1) * HD, :, F + h * HD:F + (h + 1) * HD],
                          w["L3_gnn_rel_msg"][h].rearrange("e d o -> d e o")))
        loads.append((pri[:], w["L3_gnn_rel_pri"].rearrange("(a h) e -> a h e", a=1).partition_broadcast(F)
                      .rearrange("p a h e -> p (a h) e")))
        W_IN = 16 * len(loads)

        block = ctx.enter_context(nc.Block())

        @block.sync
        def _(sp):
            ids = lambda v: v.rearrange("(p s i) -> p s i", p=P, s=SUB)
            sp.dma_start(dst_i[:], ids(dst)).then_inc(ids_in, 16)
            sp.wait_ge(zeroed, ZR)
            sp.dma_start(src_i[:, :, 0:CL], ids(src)).then_inc(ids_in, 16)
            sp.dma_start(t_idx[:, :, 0:CL], ids(etype)).then_inc(ids_in, 16)
            sp.dma_start(x_sb[:, 0:NT - 1, :], node_tiles(x[0:N - LAST, :])).then_inc(x_in, 16)
            sp.dma_start(x_sb[0:LAST, NT - 1, :], x[N - LAST:N, :]).then_inc(x_in, 16)
            with nc.allow_non_contiguous_dma("small index rows"):
                sp.dma_start(nt_i[:, 0:NT - 1], ntype[0:N - LAST].rearrange("(t p) -> p t", p=P)).then_inc(x_in, 16)
                sp.dma_start(nt_i[0:LAST, NT - 1:NT], ntype[N - LAST:N].rearrange("(p a) -> p a", a=1)).then_inc(x_in, 16)
                dv = dst.rearrange("(q i) -> q i", i=CL)
                sp.dma_start(joins_i[0:1, 0, :], dv[:, 0:1].rearrange("q a -> a q")).then_inc(oob_in, 16)
                sp.dma_start(joins_i[0:1, 1, :], dv[:, CL - 1:CL].rearrange("q a -> a q")).then_inc(oob_in, 16)
            with nc.allow_non_contiguous_dma("weights"):
                for d, s in loads:
                    sp.dma_start(d, s).then_inc(w_in, 16)
            for r in range(SUB):
                flat = agg_d[r].rearrange("(p a) f -> p (a f)", p=P)
                for o in range(0, flat.shape[1], COLS * F):
                    n = min(COLS * F, flat.shape[1] - o)
                    sp.dma_start(flat[:, o:o + n], zeros[:, 0:n]).then_inc(agg_z, 16)

            with loop(sp, 0, NBAT - 1, 2) as b:
                for i in range(2):
                    sp.wait_ge(l_b, b + (i + 1))
                    sp.dma_start(node_tiles(tab_b)[:, bass.ds((b + i) * NB, NB), :], bst[i][:]).then_inc(l_out[i], 16)
            sp.wait_ge(l_a, NBAT + 1)
            sp.dma_start(node_tiles(tab_a), side[:]).then_inc(l_ao, 16)

            def load_attr(t, tp, first):
                if not first:
                    sp.wait_ge(a_red, t * KS - KS + 1)
                sp.dma_start(at[tp][:].rearrange("p s k f -> p s (k f)"),
                             chains(attr)[:, :, bass.ds(t * (KS * F), KS * F)]).then_inc(a_ld[tp], 16)
            each_iteration(sp, load_attr)

            def first_out(n):
                sp.wait_ge(fr, 16 * SUB * (n + 1))
                sp.dma_start(chains(starts_d)[:, :, 0:F], first_rows[:]).then_inc(fr_w, 16)
                sp.wait_ge(fr_w, 16 * (n + 1))

            sp.wait_ge(scat, 16 * NT)
            first_out(0)

            def edge_io(c, side_done, run_done, run_d, width, with_side):
                def load(t, tp):
                    sp.dma_start(edge0[tp][:].rearrange("p s k f -> p s (k f)"),
                                 chains(starts_d)[:, :, bass.ds(t * (KS * F), KS * F)]).then_inc(e_in[c][tp], 16)

                def store(t, tp):
                    sp.dma_start(chains(run_d)[:, :, bass.ds(t * (KS * width), KS * width)],
                                 run_view(tp, width).rearrange("p s k f -> p s (k f)")).then_inc(r_out[c][tp], 16)

                def body(t, tp):
                    if with_side:
                        sp.wait_ge(side_done, t * KS)
                        load(t + 1, 1 - tp)
                    sp.wait_ge(run_done, t * KS)
                    store(t - 1, 1 - tp)

                if with_side:
                    load(0, 0)
                    load(1, 1)
                with loop(sp, 1, T - 3, 2) as t:
                    body(t, 1)
                    body(t + 1, 0)
                body(T - 2, 1)
                sp.wait_ge(run_done, (T - 1) * KS)
                store(T - 2, 1)
                sp.wait_ge(run_done, T * KS)
                store(T - 1, 0)
                for tp in range(2):
                    sp.wait_ge(r_out[c][tp], 16 + 16 * ((T + 1 - tp) // 2))

            def carry_out(n, car, width):
                sp.wait_ge(k_row, n + 1)
                sp.dma_start(car[0:NC, :].rearrange("(c p) f -> p c f", p=P), full[:, :, 0:width]).then_inc(k_out, 16)
                sp.dma_start(car[NC:NC + 1, :], neutral[0:1, 0:width]).then_inc(k_out, 16)

            edge_io("b", b_a, b_s, run0, F, True)
            carry_out(0, car0, F)

            def agg_in(b, bp):
                for r in range(SUB):
                    sp.dma_start(ac[bp][:, r, :, :], node_tiles(agg_d[r][0:NP, :])[:, bass.ds(b * NB, NB), :]
                                 ).then_inc(n_ac[bp], 16)

            def table_out(c, b, table):
                sp.wait_ge(n_use[c], b + 1)
                sp.dma_start(node_tiles(table)[:, bass.ds(b * NB, NB), :], x_sb[:, bass.ds(b * NB, NB), :]
                             ).then_inc(n_out[c], 16)

            for r in range(SUB):
                sp.wait_ge(a_sc[r], 16 * NG)
            agg_in(0, 0)
            agg_in(1, 1)
            with loop(sp, 0, NBAT - 3, 2) as b:
                for i in range(2):
                    table_out("1", b + i, tab_x2)
                    agg_in(b + i + 2, i)
            for b in range(NBAT - 2, NBAT):
                table_out("1", b, tab_x2)

            edge_io("c", None, c_s, run2, F, False)
            carry_out(1, car2, F)

            t_rows = tab_t.rearrange("(t p e) f -> p t (e f)", p=P, e=ET)
            with loop(sp, 0, NT - 1, 2) as n:
                for i in range(2):
                    sp.wait_ge(ta3, n * 2 + (2 * i + 4))
                    sp.dma_start(t_rows[:, bass.ds(n + i, 1), :], trow[i][:].rearrange("p e f -> p (e f)").unsqueeze(1)
                                 ).then_inc(t_o[i], 16)
            sp.wait_ge(tq, NT)
            sp.dma_start(node_tiles(tab_q), side[:]).then_inc(n_out["2"], 16)
            sp.wait_ge(scat, 2 * 16 * NT)
            first_out(1)
            edge_io("d", d_q, d_acc, run3, ROW3, True)
            carry_out(2, car3, ROW3)

            sp.wait_ge(n_use["3"], NBAT)
            sp.dma_start(node_tiles(out[0:N - LAST, :]), x_sb[:, 0:NT - 1, :]).then_inc(o_out, 16)
            sp.dma_start(out[N - LAST:N, :], x_sb[0:LAST, NT - 1, :]).then_inc(o_out, 16)
            sp.wait_ge(o_out, 32)

        @block.gpsimd
        def _(pool):
            pool.memset(ident[:], 0.0).then_inc(cst_p, 1)
            pool.memset(upper[:], 1.0).then_inc(cst_p, 1)
            pool.iota(iota_i[:], [[1, P]], base=0, channel_multiplier=0).then_inc(cst_p, 1)
            pool.iota(spare_i[:], [[0, 1]], base=NP, channel_multiplier=1).then_inc(cst_p, 1)
            pool.wait_ge(cst_p, 4)
            pool.affine_select(out=ident[:], in_=ident[:], compare_op=ALU.not_equal, fill=1.0, base=0,
                               pattern=[[-1, P]], channel_multiplier=1).then_inc(cst_p, 1)
            pool.affine_select(out=upper[:], in_=upper[:], compare_op=ALU.is_ge, fill=0.0, base=-1,
                               pattern=[[1, P]], channel_multiplier=-1).then_inc(cst_p, 1)

            pool.wait_ge(agg_z, AGG_Z)

            def scatter_add(t, tp, first):
                for k in range(KS):
                    n = t * KS + k
                    pool.wait_ge(a_row, n + 1)
                    pool.nop(nofuse=True)
                    pool.wait_ge(a_idx, n + 1)
                    pool.nop(nofuse=True)
                    for r in range(SUB):
                        if not (first and k == 0):
                            pool.wait_ge(a_sc[r], n * 16)
                            pool.nop(nofuse=True)
                        pool.indirect_dma_start(
                            agg_d[r], rows(agg_d[r], ag_idx[:, k, r:r + 1]), sums[:, k, r, :], None,
                            bounds_check=AGR - 1, oob_is_err=True, compute_op=ALU.add).then_inc(a_sc[r], 16)
            each_iteration(pool, scatter_add)

            def to_starts(n, table, table_ready, ready):
                pool.wait_ge(table_ready, ready)
                pool.wait_ge(a_done, 1)
                pool.wait_ge(e0_z, 16 * T)
                if n:
                    pool.wait_ge(fr_w, 16)
                    for tp in range(2):
                        pool.wait_ge(e_in["b"][tp], 16 * ((T + 1 - tp) // 2))
                for i in range(SUB):
                    pool.indirect_dma_start(first_rows[:, i, :], None, table, rows(table, first_i[:, i:i + 1])
                                            ).then_inc(fr, 16)
                for t in range(NT):
                    pool.indirect_dma_start(starts_d, rows(starts_d, start_x[:, t:t + 1]), side[:, t, :], None,
                                            bounds_check=E - 1, oob_is_err=False).then_inc(scat, 16)

            to_starts(0, tab_a, l_ao, 16)
            for i in range(2):
                pool.wait_ge(l_out[i], 16 + 8 * NBAT)

            def gathers(c, table, width, staged, per, used):
                def body(t, tp, first):
                    pool.wait_ge(staged, (t + 1) * per)
                    pool.nop(nofuse=True)
                    for k in range(KS):
                        if not first:
                            pool.wait_ge(used, t * KS + (k - KS + 1))
                            pool.nop(nofuse=True)
                        for s in range(SUB):
                            pool.indirect_dma_start(gat[:, k, s, 0:width], None, table,
                                                    rows(table, gi[tp][:, s, k:k + 1])).then_inc(g_in[c][k], 16)
                each_iteration(pool, body)

            def node_rows(c, run_d, car, width, n):
                def batch(b, bp):
                    pool.wait_ge(n_st[c], b * 2 + 2)
                    pool.nop(nofuse=True)
                    for i in range(NB):
                        pool.indirect_dma_start(r1[bp][:, i, 0:width], None, run_d,
                                                rows(run_d, est[bp][:, i:i + 1])).then_inc(n_r[c][bp], 16)
                        pool.indirect_dma_start(r2[bp][:, i, 0:width], None, car,
                                                rows(car, cst[bp][:, i:i + 1])).then_inc(n_r[c][bp], 16)
                tag = {"1": "b", "2": "c", "3": "d"}[c]
                for tp in range(2):
                    pool.wait_ge(r_out[tag][tp], 16 + 16 * ((T + 1 - tp) // 2))
                pool.wait_ge(k_out, 32 * (n + 1))
                batch(0, 0)
                batch(1, 1)
                with loop(pool, 2, NBAT - 1, 2) as b:
                    for i in range(2):
                        pool.wait_ge(n_use[c], b + (i - 1))
                        pool.nop(nofuse=True)
                        batch(b + i, i)

            gathers("b", tab_b, F, b_st, 3, b_u)
            node_rows("1", run0, car0, F, 0)
            pool.wait_ge(n_out["1"], 16 * NBAT)
            gathers("c", tab_x2, F, c_st, 2, c_s)
            node_rows("2", run2, car2, F, 1)
            to_starts(1, tab_q, n_out["2"], 16)
            for i in range(2):
                pool.wait_ge(t_o[i], 16 + 8 * NT)
            gathers("d", tab_t, 2 * F, d_st, 3, d_wm)
            node_rows("3", run3, car3, ROW3, 2)

        @block.scalar
        def _(act):
            act.wait_ge(zeroed, ZR)
            act.wait_ge(x_in, 64)

            def stage_x(b):
                act.activation(xst[:], x_sb[:, bass.ds(b * NB, NB), :], ACT.Copy).then_inc(l_st, 1)

            stage_x(0)
            with loop(act, 0, NBAT - 1, 2) as b0:
                for i in range(2):
                    b = b0 + i
                    act.wait_ge(l_tr, b + 1)
                    stage_x(b + 1)
                    act.activation(xTs[i][:, 0:4, :], pair[0][0:F, 0:512].rearrange("p (c n) -> p c n", c=4),
                                   ACT.Copy).then_inc(l_ev, 1)
                    act.activation(xTs[i][:, 4:NB, :], pair[0][0:F, 512:512 + (NB - 4) * P]
                                   .rearrange("p (c n) -> p c n", n=P), ACT.Copy).then_inc(l_ev, 1)
                    act.wait_ge(l_mm, b + 1)
                    act.wait_ge(l_out[i], b * 8 + (16 if i == 0 else 8))
                    act.activation(bst[i][:], pair[1][:, 0:NB * P].rearrange("p (c n) -> p c n", n=P)[:, :, F:2 * F],
                                   ACT.Copy).then_inc(l_b, 1)

            def stage_a(t, tp):
                cs = bass.ds(t * KS, KS)
                act.activation(st_hi[tp][:], s_hi[:, :, cs], ACT.Copy, scale=float(P)).then_inc(a_st, 1)
                act.activation(st_lo[tp][:], s_lo[:, :, cs], ACT.Copy).then_inc(a_st, 1)
                act.activation(st_dh[tp][:], d_hi[:, :, cs], ACT.Copy).then_inc(a_st, 1)
                act.activation(st_dl[tp][:], d_lo[:, :, cs], ACT.Copy).then_inc(a_st, 1)
                act.activation(st_s[tp][:], src_i[:, :, cs], ACT.Copy).then_inc(a_st, 1)
                act.activation(st_d[tp][:], src_i[:, :, cs], ACT.Identity, bias=spare[:, 0:1], scale=-1.0
                               ).then_inc(a_st, 1)

            act.wait_ge(prep, 1)
            stage_a(0, 0)

            def phase_a(t, tp, first):
                act.dma_start(starts_d.rearrange("(p j) f -> p (j f)", p=P)[:, bass.ds(t * (COLS * F), COLS * F)],
                              zeros[:]).then_inc(e0_z, 16)
                for k in range(KS):
                    n = t * KS + k
                    act.wait_ge(a_eq, n + 1)
                    if not (first and k < 2):
                        act.wait_ge(a_red, n - 1)
                    act.activation(same_bf[(tp + k) % 2][:], same[(tp + k) % 2][:], ACT.Copy).then_inc(a_sb, 1)
                    act.wait_ge(a_red, n + 1)
                    if not first:
                        for r in range(SUB):
                            act.wait_ge(a_sc[r], n * 16 - 16 * (KS - 1))
                    act.activation(sums[:, k, :, :],
                                   bank[(tp + k) % 2][:, 0:SUB * AGW].rearrange("p (c f) -> p c f", c=SUB),
                                   ACT.Copy).then_inc(a_row, 1)
                    if k == 2:
                        if not first:
                            act.wait_ge(a_idx, t * KS)
                        stage_a(t + 1, 1 - tp)
            each_iteration(act, phase_a)

            def stage(c, st, index, t, tp, with_pen):
                cs = bass.ds(t * KS, KS)

                act.activation(gi[tp][:], index[:, :, cs], ACT.Copy).then_inc(st, 1)
                act.activation(ct[tp][:], cont[:, :, cs], ACT.Copy).then_inc(st, 1)
                if with_pen:
                    act.activation(pn[tp][:], cont[:, :, cs], ACT.Copy, bias=-FAR, scale=FAR).then_inc(st, 1)

            act.wait_ge(a_done, 1)
            stage("b", b_st, src_i, 0, 0, True)

            def phase_b(t, tp, first):
                for k in range(KS):
                    n = t * KS + k
                    act.wait_ge(b_tr, n + 1)
                    if not (first and k < 2):
                        act.wait_ge(b_msg, n - 1)
                    q = (tp + k) % 2
                    act.activation(hT[q][:, 0:2, :], bank[q][:, 0:256].rearrange("p (c n) -> p c n", c=2),
                                   ACT.Relu).then_inc(b_h, 1)
                    act.activation(hT[q][0:F, 2, :], bank[q][0:F, 256:384], ACT.Relu).then_inc(b_h, 1)
                    if k == 2:
                        if not first:
                            act.wait_ge(b_s, t * KS)
                        stage("b", b_st, src_i, t + 1, 1 - tp, True)
            each_iteration(act, phase_b)

            def stage_nodes(c, b, bp):
                act.activation(est[bp][:], end_x[:, bass.ds(b * NB, NB)], ACT.Copy).then_inc(n_st[c], 1)
                act.activation(cst[bp][:], car_x[:, bass.ds(b * NB, NB)], ACT.Copy).then_inc(n_st[c], 1)

            def root(c, b, i):
                act.wait_ge(n_s[c], b)
                act.activation(sm[:, 2, :], sm[:, 1, :], ACT.Sqrt, bias=eps_c[:, 0:1], scale=1.0 / F
                               ).then_inc(n_a2[c], 1)

            def node_loop(c, body):
                stage_nodes(c, 0, 0)
                stage_nodes(c, 1, 1)
                with loop(act, 0, NBAT - 1, 2) as b:
                    for i in range(2):
                        body(b + i)
                        act.wait_ge(n_r[c][i], b * (16 * NB) + 32 * NB)
                        stage_nodes(c, b + (i + 2), i)

            def stage1(b):
                root("1", b * 2 + 1, 0)
                act.wait_ge(n_m["1"], b * 3 + 1)
                act.activation(cT[:, 0:4, :], pair[0][:, 0:512].rearrange("p (c n) -> p c n", c=4),
                               ACT.Copy).then_inc(n_a2["1"], 1)
                act.activation(cT[:, 4:NB, :], pair[0][:, 512:NB * P].rearrange("p (c n) -> p c n", n=P),
                               ACT.Copy).then_inc(n_a2["1"], 1)
                act.wait_ge(n_m["1"], b * 3 + 2)
                act.activation(hTn[:, 0:4, :], pair[1][0:F, 0:512].rearrange("p (c n) -> p c n", c=4),
                               ACT.Relu, bias=c_1[:, 0:1]).then_inc(n_a2["1"], 1)
                act.activation(hTn[:, 4:NB, :], pair[1][0:F, 512:NB * P].rearrange("p (c n) -> p c n", n=P),
                               ACT.Relu, bias=c_1[:, 0:1]).then_inc(n_a2["1"], 1)
                root("1", b * 2 + 2, 1)
            node_loop("1", stage1)

            act.wait_ge(n_use["1"], NBAT)
            stage("c", c_st, src_i, 0, 0, False)

            def phase_c(t, tp, first):
                if not first:
                    act.wait_ge(c_s, t * KS)
                stage("c", c_st, src_i, t + 1, 1 - tp, False)
            each_iteration(act, phase_c)

            def stage2(b):
                act.wait_ge(n_m["2"], b * 2 + 1)
                act.activation(cT[0:F, 0:4, :], pair[0][0:F, 0:512].rearrange("p (c n) -> p c n", c=4),
                               ACT.Copy).then_inc(n_a2["2"], 1)
                act.activation(cT[0:F, 4:NB, :], pair[0][0:F, 512:NB * P].rearrange("p (c n) -> p c n", n=P),
                               ACT.Copy).then_inc(n_a2["2"], 1)
                root("2", b + 1, 0)
            node_loop("2", stage2)

            def evac_xm(n, i):
                act.wait_ge(tp1, n + 1)
                act.activation(xmT[i][:], bank[i][:, 0:2 * P].rearrange("p (a n) -> p a n", a=2), ACT.Copy
                               ).then_inc(ta1, 1)

            def evac_kv(n, i):
                act.wait_ge(tp2, n + 1)
                act.activation(kvT[i][:], pair[0][:, 0:P], ACT.Copy).then_inc(ta2, 1)

            evac_xm(0, 0)
            evac_kv(0, 0)
            with loop(act, 0, NT - 1, 2) as n:
                for i in range(2):
                    evac_xm(n + (i + 1), 1 - i)
                    evac_kv(n + (i + 1), 1 - i)
                    act.wait_ge(tp4, n + (i + 1))
                    act.wait_ge(t_o[i], n * 8 + 16)
                    for hb in range(2):
                        act.activation(trow[i][:, 4 * hb:4 * hb + 4, :],
                                       pair[1][:, 512 * hb:512 * hb + 512].rearrange("p (e f) -> p e f", e=4),
                                       ACT.Copy).then_inc(ta3, 1)

            stage("d", d_st, t_idx, 0, 0, True)

            def phase_d(t, tp, first):
                for k in range(KS):
                    n = t * KS + k
                    q = (tp + k) % 2
                    act.wait_ge(d_dm, n * 2 + 2)
                    if not (first and k < 2):
                        act.wait_ge(d_acc, n - 1)
                    act.activation(al[q][:], dm[q][:, 0, :, :], ACT.Exp).then_inc(d_ex, 1)
                    act.activation(wm[q][:, :, :, HD], dm[q][:, 1, :, :], ACT.Exp).then_inc(d_ex, 1)
                    if k == 2:
                        if not first:
                            act.wait_ge(d_acc, t * KS)
                        stage("d", d_st, t_idx, t + 1, 1 - tp, True)
            each_iteration(act, phase_d)

            act.wait_ge(k_sc, 1)
            act.activation(fullT[0:H * HR, 2:4, :], fullT[0:H * HR, 2:4, :], ACT.Exp).then_inc(k_ev, 1)

            def stage3(b):
                act.wait_ge(n_v["3"], b * 2 + 1)
                act.activation(s4[:, 3:5, :, :], s4[:, 1:3, :, :], ACT.Exp).then_inc(n_a2["3"], 1)
                act.wait_ge(n_m["3"], b * 2 + 1)
                act.activation(cT[0:F, 0:4, :], pair[0][0:F, 0:512].rearrange("p (c n) -> p c n", c=4),
                               ACT.Copy).then_inc(n_a2["3"], 1)
                act.activation(cT[0:F, 4:NB, :], pair[0][0:F, 512:NB * P].rearrange("p (c n) -> p c n", n=P),
                               ACT.Copy).then_inc(n_a2["3"], 1)
                root("3", b + 1, 0)
            node_loop("3", stage3)

        @block.tensor
        def _(pe):
            def transposes(dst_pair, source, m):
                pe.nop(nofuse=True)
                for i in range(NB):
                    last = pe.transpose(dst_pair[0:m, i * P:(i + 1) * P], source[:, i, 0:m], ident[:])
                return last

            pe.wait_ge(cst_v, 3)
            pe.wait_ge(pre, 7)
            pe.wait_ge(wprep, 2)
            for e in range(ET):
                last = pe.matmul(bank[0][0:F, e * F:(e + 1) * F], rat[:, e, :], rat[:, e, :], start=True, stop=True)
            last.then_inc(prep_m, 1)
            pe.matmul(bank[1][0:F, 0:1], w1u_1[:], u_col[:], start=True, stop=True).then_inc(prep_m, 1)
            pe.wait_ge(wprep, 3)
            for o in range(0, NC, 512):
                n = min(512, NC - o)
                last = pe.matmul(pair[0][:, o:o + n], ones[0:1, :], joins[0:1, 0, o:o + n], start=True, stop=True)
            last.then_inc(prep_m, 1)
            pe.wait_ge(wprep, 5)

            def x_products(b, i):
                pe.wait_ge(l_ev, b * 2 + 2)
                pe.wait_ge(l_a, b + 1)
                for c in range(NB):
                    last = pe.matmul(pair[1][:, c * P:(c + 1) * P], xTs[i][:, c, :],
                                     w_ab[:].rearrange("p a f -> p (a f)"), start=True, stop=True)
                last.then_inc(l_mm, 1)

            with loop(pe, 0, NBAT - 1, 2) as b0:
                for i in range(2):
                    pe.wait_ge(l_st, b0 + (i + 1))
                    transposes(pair[0], xst, F).then_inc(l_tr, 1)
                    x_products(b0 + i, i)

            pe.wait_ge(l_a, NBAT + 1)
            hist = bank[2][:, 0:NT]
            pe.matmul(hist, zero_bf[:], zero_bf[:, 0:NT], start=True, stop=False, skip_group_check=True)

            def rank_rows(t, tp, k, first):
                q = (tp + k) % 2
                n = t * KS + k
                if not (first and k < 2):
                    pe.wait_ge(a_eq, n - 1)
                for s in range(SUB):
                    o = pair[q][:, s * P:(s + 1) * P]
                    pe.matmul(o, spread(st_hi[tp][:, s, k], P), idn_bf[:],
                              start=True, stop=False)
                    last = pe.matmul(o, spread(st_lo[tp][:, s, k], P), idn_bf[:],
                                     start=False, stop=True)
                last.then_inc(a_bc, 1)

            def reduce_cols(t, tp, k, early, first_ever):
                q = (tp + k) % 2
                n = t * KS + k
                if k == 0:
                    pe.wait_ge(a_ld[tp], sides(t, tp))
                pe.wait_ge(a_su, n + 1)
                pe.wait_ge(a_oh, n * 2 + 2)
                pe.wait_ge(a_sb, n + 1)
                if not early:
                    pe.wait_ge(a_row, n - 1)
                if not first_ever:
                    pe.wait_ge(a_tt, n)
                for s in range(SUB):
                    o = s * AGW
                    pe.matmul(bank[q][:, o:o + F], same[q][:, s, :], at[tp][:, s, k, :], start=True, stop=True)
                    pe.matmul(bank[q][:, o + F:o + AGW], same_bf[q][:, s, :], ones_bf[:, 0:1], start=True, stop=True)
                    pe.matmul(bank[3][:, s:s + 1], before[q][:, s, :], ones_bf[:, 0:1],
                              start=True, stop=True)
                    last = pe.matmul(hist, oh_lo[q][:, s, :], oh_hi[q][:, s, :], start=False, stop=False,
                                     skip_group_check=True)
                last.then_inc(a_red, 1)

            def phase_a(t, tp, first):
                pe.wait_ge(a_st, t * 6 + 6)
                for k in range(KS):
                    rank_rows(t, tp, k, first)
                    if k:
                        reduce_cols(t, tp, k - 1, first and k - 1 < 2, first and k == 1)
                reduce_cols(t, tp, KS - 1, False, False)
            each_iteration(pe, phase_a)
            pe.matmul(hist, zero_bf[:], zero_bf[:, 0:NT], start=False, stop=True,
                      skip_group_check=True).then_inc(a_hist, 1)

            pe.wait_ge(a_pre, 1)
            pe.wait_ge(a_row, NG)
            pe.matmul(bank[0][:, 0:NT], upper[:], deg[:], start=True, stop=True)
            pe.matmul(bank[1][:, 0:NT], ones[:], deg[:], start=True, stop=True).then_inc(a_hist, 1)
            pe.wait_ge(a_done, 1)

            def rows_T(t, tp, k, early):
                q = (tp + k) % 2
                n = t * KS + k
                pe.wait_ge(b_u, n + 1)
                if not early:
                    pe.wait_ge(b_h, n * 2 - 2)
                pe.nop(nofuse=True)
                for i in range(2):
                    pe.transpose(bank[q][:, i * P:(i + 1) * P],
                                 ub[q][:, 2 * i:2 * i + 2, :].rearrange("p s f -> p (s f)"), ident[:])
                pe.transpose(bank[q][0:F, 2 * P:3 * P], ub[q][:, 4, :], ident[:]).then_inc(b_tr, 1)

            def messages(t, tp, k, early):
                q = (tp + k) % 2
                n = t * KS + k
                pe.wait_ge(b_h, n * 2 + 2)
                if not early:
                    pe.wait_ge(b_s, n - 1)
                o = bank[2 + q]
                for i in range(2):
                    pe.matmul(o[:, i * P:(i + 1) * P], hT[q][:, i, :], w2_0[:].rearrange("p a f -> p (a f)"),
                              start=True, stop=True)
                pe.matmul(o[:, 2 * P:2 * P + F], hT[q][0:F, 2, :], w2_0[0:F, 0, :], start=True, stop=True
                          ).then_inc(b_msg, 1)

            def phase_b(t, tp, first):
                for k in range(KS):
                    rows_T(t, tp, k, first and k < 2)
                    if k:
                        messages(t, tp, k - 1, first and k - 1 < 2)
                    elif not first:
                        messages(t - 1, 1 - tp, KS - 1, False)
            each_iteration(pe, phase_b)
            messages(T - 1, 0, KS - 1, False)

            def carry(n, width, parts):
                pe.wait_ge(k_tl, n + 1)
                for j in range(parts):
                    for s in range(SUB):
                        last = pe.transpose(pair[j][0:width, s * P:(s + 1) * P], tails[:, s, j, 0:width], ident[:])
                last.then_inc(k_tr, 1)
                pe.wait_ge(k_fu, n + 1)
                for j in range(parts):
                    for c in range(SUB):
                        last = pe.transpose(bank[j][:, c * width:(c + 1) * width],
                                            fullT[0:width, j, c * P:(c + 1) * P], ident[0:width, 0:width])
                last.then_inc(k_tb, 1)

            carry(0, F, 1)
            with loop(pe, 0, NBAT) as b:
                pe.wait_ge(n_v["1"], b + 1)
                transposes(pair[0], comb, 2 * F).then_inc(n_m["1"], 1)
                pe.wait_ge(n_a2["1"], b * 6 + 3)
                for i, n in ((0, 4), (4, NB - 4)):
                    last = pe.matmul(pair[1][0:F, i * P:(i + n) * P], w1_1[:],
                                     cT[:, i:i + n, :].rearrange("p c n -> p (c n)"), start=True, stop=True)
                last.then_inc(n_m["1"], 1)
                pe.wait_ge(n_a2["1"], b * 6 + 5)
                for i in range(NB):
                    last = pe.matmul(bank[0][:, i * F:(i + 1) * F], hTn[:, i, :], w2_1[:], start=True, stop=True)
                last.then_inc(n_m["1"], 1)

            carry(1, F, 1)
            with loop(pe, 0, NBAT) as b:
                pe.wait_ge(n_v["2"], b + 1)
                transposes(pair[0], yb, F).then_inc(n_m["2"], 1)
                pe.wait_ge(n_a2["2"], b * 3 + 2)
                for i in range(NB):
                    last = pe.matmul(bank[0][:, i * (F + 3):(i + 1) * (F + 3)], cT[0:F, i, :], w_2[:],
                                     start=True, stop=True)
                last.then_inc(n_m["2"], 1)

            def xm_T(n, i):
                pe.wait_ge(tv, n + 1)
                pe.nop(nofuse=True)
                for a in range(2):
                    last = pe.transpose(bank[i][:, a * P:(a + 1) * P],
                                        xm[i][:, 2 * a:2 * a + 2, :].rearrange("p a f -> p (a f)"), ident[:])
                last.then_inc(tp1, 1)

            def project(n, i):
                pe.wait_ge(ta1, n + 1)
                for a in range(2):
                    pe.matmul(pair[0][:, 0:P], w_kvq[:, a, 0:2 * F], xmT[i][:, a, :], start=(a == 0), stop=(a == 1))
                for a in range(2):
                    last = pe.matmul(pair[0][:, 512:512 + F], xmT[i][:, a, :], w_kvq[:, a, 2 * F:3 * F],
                                     start=(a == 0), stop=(a == 1))
                last.then_inc(tp2, 1)

            xm_T(0, 0)
            project(0, 0)
            with loop(pe, 0, NT - 1, 2) as n:
                for i in range(2):
                    xm_T(n + (i + 1), 1 - i)
                    pe.wait_ge(ta2, n + (i + 1))
                    pe.wait_ge(ta3, n * 2 + (2 * i + 2))
                    for g in range(2):
                        last = pe.matmul(pair[1][:, g * 512:(g + 1) * 512], kvT[i][:],
                                         w_rel[:, 4 * g:4 * g + 4, :].rearrange("p e f -> p (e f)"),
                                         start=True, stop=True)
                    last.then_inc(tp4, 1)
                    pe.wait_ge(tq, n + (i + 1))
                    project(n + (i + 1), 1 - i)

            carry(2, H * HR, 2)
            with loop(pe, 0, NBAT) as b:
                pe.wait_ge(n_v["3"], b * 2 + 2)
                transposes(pair[0], yb, F).then_inc(n_m["3"], 1)
                pe.wait_ge(n_a2["3"], b * 4 + 3)
                for i in range(NB):
                    o = pair[1][:, i * 256:(i + 1) * 256] if i < 4 else pair[0][:, (i - 4) * 256:(i - 3) * 256]
                    last = pe.matmul(o, cT[0:F, i, :], w_a3[:].rearrange("p a f -> p (a f)"),
                                     start=True, stop=True)
                last.then_inc(n_m["3"], 1)

        @block.vector
        def _(v):
            TT = v.tensor_tensor
            TS = v.tensor_scalar
            tokens = iter(range(20))

            def token():
                i = next(tokens)
                return v.memset(marks[:, i:i + 1], 0.0)

            v.memset(zeros[:], 0.0).then_inc(zeroed, 1)
            v.memset(x_sb[:, NT - 1:NT + NB, :], 0.0).then_inc(zeroed, 1)
            v.memset(rat[:], 0.0).then_inc(zeroed, 1)
            v.memset(w_rel[:], 0.0).then_inc(zeroed, 1)
            v.memset(w2_0[:], 0.0).then_inc(zeroed, 1)
            v.memset(src_i[:], 0).then_inc(zeroed, 1)
            v.memset(t_idx[:], 0).then_inc(zeroed, 1)
            v.memset(cont[:], 0.0).then_inc(zeroed, 1)
            v.memset(nt_i[:], 0).then_inc(zeroed, 1)
            for sems in (r_out["b"], r_out["c"], r_out["d"], t_o, l_out):
                for q in sems:
                    token().then_inc(q, 16)
            token().then_inc(ta3, 2)
            token().then_inc(l_a, 1)
            v.memset(ones[:], 1.0).then_inc(cst_v, 1)
            v.memset(ones_bf[:], 1.0).then_inc(pre, 1)
            v.memset(zero_bf[:], 0.0).then_inc(pre, 1)
            v.memset(eps_c[:], LN_EPS).then_inc(pre, 1)
            v.memset(end_x[:], 0).then_inc(pre, 1)
            v.memset(nmask[:, :, NT:NT + 1], 0.0).then_inc(pre, 1)
            v.memset(car_x[:], 0).then_inc(pre, 1)
            v.memset(joins[:], 0.0).then_inc(pre, 1)
            v.wait_ge(pre, 7)
            link = Link(v, ch_pre, 0)
            v.wait_ge(cst_p, 6)
            v.tensor_copy(idn_bf[:], ident[:]).then_inc(cst_v, 1)
            v.tensor_copy(iota_bf[:], iota_i[:]).then_inc(cst_v, 1)
            link(v.tensor_copy(spare[:], spare_i[:]))
            v.wait_ge(zeroed, ZR)
            v.wait_ge(ids_in, 48)
            for ids_, mask, op, parts in ((src_i, 7, ALU.logical_shift_right, s_hi), (src_i, 127, ALU.bitwise_and, s_lo),
                                          (dst_i, 7, ALU.logical_shift_right, d_hi),
                                          (dst_i, 127, ALU.bitwise_and, d_lo)):
                link(TS(part_i[:], ids_[:, :, 0:CL], mask, None, op))
                link(v.tensor_copy(parts[:, :, 0:CL], part_i[:]))
                link(v.memset(parts[:, :, CL:CL + KS], 0))
            TT(cont[:, :, 1:CL], dst_i[:, :, 1:CL], dst_i[:, :, 0:CL - 1], ALU.is_equal).then_inc(prep, 1)
            link(v.tensor_copy(first_i[:], dst_i[:, :, 0]))
            link(TS(part_i[:], src_i[:, :, 0:CL], float(ET), None, ALU.mult))
            link(TT(t_idx[:, :, 0:CL], part_i[:], t_idx[:, :, 0:CL], ALU.add))
            v.wait_ge(w_in, W_IN)
            link(TT(w_ab[:, 0, :], w_ab[:, 0, :], w_ab[:, 1, :], ALU.subtract))
            link(TS(pri[:], pri[:], 1.0 / float(HD) ** 0.5, None, ALU.mult))
            v.wait_ge(x_in, 64)
            for ty in range(NTY):
                TS(nmask[:, ty, 0:NT], nt_i[:], float(ty), None, ALU.is_equal).then_inc(wprep2, 1)
            token().then_inc(wprep, 2)
            v.wait_ge(oob_in, 32)
            link(TT(joins[0:1, 0, 1:NC], joins_i[0:1, 0, 1:NC], joins_i[0:1, 1, 0:NC - 1], ALU.is_equal))
            link(TT(joins[0:1, 1, :], joins_i[0:1, 0, :], joins_i[0:1, 1, :], ALU.is_equal))
            link(TT(joins[0:1, 0, :], joins[0:1, 0, :], joins[0:1, 1, :], ALU.mult))
            token().then_inc(wprep, 1)
            v.wait_ge(prep_m, 3)
            TT(w_rel[0:F, :, 0:F].rearrange("p e (h d) -> p e h d", h=H),
               bank[0][0:F, :].rearrange("p (e h d) -> p e h d", e=ET, h=H),
               spread(pri[:].rearrange("p h e -> p e h"), HD), ALU.mult).then_inc(wprep, 1)
            TT(c_1[:], bank[1][0:F, 0:1], b1_1[:], ALU.add).then_inc(wprep2, 1)
            link(v.tensor_copy(fj[:], pair[0][:, 0:NC]))
            TS(fjp[:], fj[:], 1.0, FAR, ALU.subtract, ALU.mult).then_inc(wprep, 1)

            with loop(v, 0, NBAT) as b:
                v.wait_ge(l_b, b + 1)
                TT(side[:, bass.ds(b * NB, NB), :],
                   pair[1][:, 0:NB * P].rearrange("p (c n) -> p c n", n=P)[:, :, 0:F],
                   spread_mid(b1_0[:], NB), ALU.add).then_inc(l_a, 1)

            v.wait_ge(l_a, NBAT + 1)
            for i in range(2):
                v.wait_ge(l_out[i], 16 + 8 * NBAT)

            def compare(t, tp, k, first):
                q = (tp + k) % 2
                n = t * KS + k
                early = first and k < 2
                v.wait_ge(a_bc, n + 1)
                if not early:
                    v.wait_ge(a_red, n - 1)
                TT(same[q][:], pair[q][:, 0:SUB * P].rearrange("p (s n) -> p s n", s=SUB),
                   spread(st_s[tp][:, :, k], P), ALU.is_equal).then_inc(a_eq, 1)
                TT(oh_lo[q][:], spread_mid(iota_bf[:], SUB), spread(st_dl[tp][:, :, k], P), ALU.is_equal
                   ).then_inc(a_oh, 1)
                v.wait_ge(a_eq, n + 1)
                TT(before[q][:], same[q][:], spread_mid(upper[:], SUB), ALU.mult).then_inc(a_su, 1)
                TT(oh_hi[q][:], spread_mid(iota_bf[:, 0:NT], SUB), spread(st_dh[tp][:, :, k], NT), ALU.is_equal
                   ).then_inc(a_oh, 1)

            def table_rows(t, tp, k, first):
                n = t * KS + k
                q = (tp + k) % 2
                v.wait_ge(a_red, n + 1)
                if not (first and k == 0):
                    v.wait_ge(a_idx, n)
                v.scalar_tensor_tensor(ag_t[:], bank[3][:, 0:SUB], 1.0, st_d[tp][:, :, k], ALU.min,
                                       ALU.mult).then_inc(a_tt, 1)
                if not first:
                    for r in range(SUB):
                        v.wait_ge(a_sc[r], n * 16 - 16 * (KS - 1))
                v.wait_ge(a_tt, n + 1)
                TT(ag_idx[:, k, :], ag_t[:], st_s[tp][:, :, k], ALU.add).then_inc(a_idx, 1)

            def phase_a(t, tp, first):
                v.wait_ge(a_st, t * 6 + 6)
                for k in range(KS):
                    compare(t, tp, k, first)
                    if k:
                        table_rows(t, tp, k - 1, first)
                table_rows(t, tp, KS - 1, first)
            each_iteration(v, phase_a)

            v.wait_ge(a_hist, 1)
            v.tensor_copy(deg[:], bank[2][:, 0:NT]).then_inc(a_pre, 1)
            v.wait_ge(a_hist, 2)
            W = lambda i: nwork[:, i, :]
            link(v.tensor_copy(W(0), bank[1][:, 0:NT]))
            v.tensor_tensor_scan(W(1), ones[:, 0:NT], W(0), 0.0, ALU.mult, ALU.add).then_inc(ch_pre, 1)
            link.n += 1
            v.wait_ge(ch_pre, link.n)
            link(TT(W(1), W(1), W(0), ALU.subtract))
            link(TT(W(1), W(1), bank[0][:, 0:NT], ALU.add))
            link(TT(W(2), W(1), deg[:], ALU.add))
            link(TS(W(2), W(2), -1.0, 0.0, ALU.add, ALU.max))
            link(v.tensor_copy(end_x[:, 0:NT], W(2)))
            link(TS(W(3), deg[:], 0.0, SKIP, ALU.is_equal, ALU.mult))
            link(TT(start_x[:], W(1), W(3), ALU.add))
            link(TS(dmask[:], deg[:], 1.0, None, ALU.min))
            link(TS(W(4), deg[:], 1.0, None, ALU.max))
            link(v.reciprocal(rdeg[:], W(4)))
            link(TS(W(5), W(2), -(CL - 1) / 2.0, 1.0 / CL, ALU.add, ALU.mult))
            link(v.tensor_copy(nwork_i[:], W(5)))
            link(v.tensor_copy(W(5), nwork_i[:]))
            link(TS(W(6), W(5), float(CL), None, ALU.mult))
            link(TT(W(6), W(6), W(1), ALU.is_gt))
            link(TS(W(5), W(5), -(NC + 1.0), None, ALU.add))
            link(TT(W(5), W(5), W(6), ALU.mult))
            link(TS(car_x[:, 0:NT], W(5), float(NC), None, ALU.add))
            for r in range(SUB):
                v.wait_ge(a_sc[r], 16 * NG)
            link(v.memset(zst[:], 0.0))
            link(v.memset(cur[:], 0.0))
            v.wait_ge(wprep2, NTY + 1)
            token().then_inc(a_done, 1)

            def previous(tp, k, width, first):
                if k:
                    return run_view(tp, width)[:, :, k - 1, :]
                return zst[:, :, 0:width] if first else run_view(1 - tp, width)[:, :, KS - 1, :]

            def open_max(t, tp, k, first):
                TT(p1[:], previous(tp, k, F, first), spread(pn[tp][:, :, k], F), ALU.add).then_inc(b_p1, 1)

            def run_max(t, tp, k):
                n = t * KS + k
                if k == 0:
                    v.wait_ge(r_out["b"][tp], sides(t, tp))
                v.wait_ge(b_msg, n + 1)
                v.wait_ge(b_p1, n + 1)
                TT(run_view(tp, F)[:, :, k, :], p1[:],
                   bank[2 + (tp + k) % 2][:, 0:SUB * F].rearrange("p (s f) -> p s f", s=SUB), ALU.max
                   ).then_inc(b_s, 1)

            def phase_b(t, tp, first):
                v.wait_ge(b_st, t * 3 + 3)
                v.wait_ge(e_in["b"][tp], sides(t, tp))
                for k in range(KS):
                    n = t * KS + k
                    back = (t, tp, k - 2) if k >= 2 else None if first else (t - 1, 1 - tp, k + KS - 2)
                    was_first = first and k == 2
                    if not (first and k == 0):
                        v.wait_ge(b_a, n)
                    TT(t1[:], cur[:], spread(ct[tp][:, :, k], F), ALU.mult).then_inc(b_t1, 1)
                    if back:
                        if not was_first:
                            v.wait_ge(b_s, n - 2)
                        open_max(*back, was_first)
                    v.wait_ge(b_t1, n + 1)
                    if not (first and k == 0):
                        v.wait_ge(b_u, n)
                    TT(cur[:], t1[:], edge0[tp][:, :, k, :], ALU.add).then_inc(b_a, 1)
                    if back:
                        run_max(*back)
                    v.wait_ge(g_in["b"][k], t * (16 * SUB) + 16 * SUB)
                    v.wait_ge(b_a, n + 1)
                    if not (first and k < 2):
                        v.wait_ge(b_tr, n - 1)
                    TT(ub[(tp + k) % 2][:], cur[:], gat[:, k, :, 0:F], ALU.add).then_inc(b_u, 1)
            each_iteration(v, phase_b)
            for k in (KS - 2, KS - 1):
                v.wait_ge(b_s, (T - 1) * KS + k)
                open_max(T - 1, 0, k, False)
                run_max(T - 1, 0, k)

            klink = Link(v, ch_k, 0)

            def carry(n, width, parts, run_done):
                v.wait_ge(run_done, NG)
                if parts == 1:
                    v.tensor_copy(tails[:, :, 0, 0:width], run_view(0, width)[:, :, KS - 1, :]).then_inc(k_tl, 1)
                else:
                    r = run_view(0, ROW3)[:, :, KS - 1, :].rearrange("p s (h d) -> p s h d", h=H)
                    o = tails[:].rearrange("p s a (h d) -> p s a h d", h=H)
                    klink(v.tensor_copy(o[:, :, 0], r[:, :, :, 0:HR]))
                    v.tensor_copy(o[:, :, 1], spread(r[:, :, :, HR], HR)).then_inc(k_tl, 1)
                v.wait_ge(k_tr, n + 1)
                for j in range(parts):
                    klink(v.tensor_copy(tailT[0:width, j, :].rearrange("w (p s) -> w s p", s=SUB),
                                       pair[j][0:width, 0:NC].rearrange("w (s p) -> w s p", s=SUB)))
                fT = lambda i: fullT[0:width, i, :]
                tT = lambda i: tailT[0:width, i, :]
                J0, JP = fj[0:width, :], fjp[0:width, :]
                if n == 0:
                    v.tensor_tensor_scan(fT(0), JP, tT(0), -FAR, ALU.add, ALU.max).then_inc(k_fu, 1)
                elif n == 1:
                    v.tensor_tensor_scan(fT(0), J0, tT(0), 0.0, ALU.mult, ALU.add).then_inc(k_fu, 1)
                else:
                    klink(v.tensor_tensor_scan(fT(1), JP, tT(1), -FAR, ALU.add, ALU.max))
                    klink(v.memset(fullT[0:width, 2, 0:1], -FAR))
                    klink(TT(fullT[0:width, 2, 1:NC], fullT[0:width, 1, 0:NC - 1], fjp[0:width, 1:NC], ALU.add))
                    klink(TT(fT(2), fT(2), fT(1), ALU.subtract))
                    TT(fT(3), tT(1), fT(1), ALU.subtract).then_inc(k_sc, 1)
                    v.wait_ge(k_ev, 1)
                    klink(TT(tT(0), tT(0), fT(3), ALU.mult))
                    v.tensor_tensor_scan(fT(0), fT(2), tT(0), 0.0, ALU.mult, ALU.add).then_inc(k_fu, 1)
                if n:
                    v.wait_ge(k_out, 32 * n)
                klink(v.memset(neutral[:], -FAR if n == 0 else 0.0))
                if n == 2:
                    klink(v.memset(neutral[:].rearrange("p (h d) -> p h d", h=H)[:, :, HR:HR + 1], -FAR))
                v.wait_ge(k_tb, n + 1)
                if parts == 1:
                    v.tensor_copy(full[:, :, 0:width], bank[0][:, 0:SUB * width].rearrange("p (c f) -> p c f", c=SUB)
                                  ).then_inc(k_row, 1)
                else:
                    o = full[:].rearrange("p c (h d) -> p c h d", h=H)
                    i0, i1 = [bank[j][:, 0:SUB * width].rearrange("p (c h d) -> p c h d", c=SUB, h=H) for j in (0, 1)]
                    klink(v.tensor_copy(o[:, :, :, 0:HR], i0))
                    v.tensor_copy(o[:, :, :, HR], i1[:, :, :, 0]).then_inc(k_row, 1)

            def norm(c, link, y, roots, dst):
                link(v.tensor_reduce(sm[:, 0, :], y, AX, ALU.add))
                link(TS(sm[:, 0, :], sm[:, 0, :], -1.0 / F, None, ALU.mult))
                link(TT(y, y, spread(sm[:, 0, :], F), ALU.add))
                link(TT(sq[:], y, y, ALU.mult))
                v.tensor_reduce(sm[:, 1, :], sq[:], AX, ALU.add).then_inc(n_s[c], 1)
                v.wait_ge(n_a2[c], roots)
                link(v.reciprocal(sm[:, 3, :], sm[:, 2, :]))
                return TT(dst, y, spread(sm[:, 3, :], F), ALU.mult)

            def batches(c, per, body):
                with loop(v, 0, NBAT - 1, 2) as b:
                    for i in range(2):
                        link = Link(v, ch_n[c], (b + i) * per)
                        v.wait_ge(n_r[c][i], b * (16 * NB) + 32 * NB)
                        body(b + i, i, link)
                        assert link.n == per, (c, link.n)

            def cols(a, b):
                return a[:, bass.ds(b * NB, NB)]

            def stage1(b, bp, link):
                y, xs = yb[:], x_sb[:, bass.ds(b * NB, NB), :]
                link(TT(y, r1[bp][:, :, 0:F], r2[bp][:, :, 0:F], ALU.max))
                link(TT(y, y, spread_mid(b2_0[:], NB), ALU.add))
                link(TT(y, y, spread(cols(dmask, b), F), ALU.mult))
                link(TT(y, y, xs, ALU.add))
                link(norm("1", link, y, b * 6 + 1, comb[:, :, 0:F]))
                a = ac[bp]
                v.wait_ge(n_ac[bp], b * (8 * SUB) + (16 * SUB if bp == 0 else 8 * SUB))
                for i, j in ((0, 1), (2, 3), (0, 2), (0, 4)):
                    link(TT(a[:, i], a[:, i], a[:, j], ALU.add))
                link(TS(sm[:, 4, :], a[:, 0, :, F], 1.0, None, ALU.max))
                link(v.reciprocal(sm[:, 5, :], sm[:, 4, :]))
                TT(comb[:, :, F:2 * F], a[:, 0, :, 0:F], spread(sm[:, 5, :], F), ALU.mult).then_inc(n_v["1"], 1)
                v.wait_ge(n_m["1"], b * 3 + 3)
                link(TT(y, bank[0][:, 0:NB * F].rearrange("p (c f) -> p c f", c=NB), spread_mid(b2_1[:], NB), ALU.add))
                link(TS(y, y, 0.0, None, ALU.max))
                link(TT(y, y, comb[:, :, 0:F], ALU.add))
                norm("1", link, y, b * 6 + 6, xs).then_inc(n_use["1"], 1)
                v.wait_ge(n_use["1"], b + 1)

            carry(0, F, 1, b_s)
            batches("1", 24, stage1)

            def phase_c(t, tp, first):
                v.wait_ge(c_st, t * 2 + 2)
                v.wait_ge(r_out["c"][tp], sides(t, tp))
                for k in range(KS):
                    n = t * KS + k
                    if not (first and k == 0):
                        v.wait_ge(c_s, n)
                    TT(p1[:], previous(tp, k, F, first), spread(ct[tp][:, :, k], F), ALU.mult).then_inc(c_t1, 1)
                    v.wait_ge(c_t1, n + 1)
                    v.wait_ge(g_in["c"][k], t * (16 * SUB) + 16 * SUB)
                    TT(run_view(tp, F)[:, :, k, :], p1[:], gat[:, k, :, 0:F], ALU.add).then_inc(c_s, 1)
            each_iteration(v, phase_c)

            def stage2(b, bp, link):
                y, z, xs = yb[:], zb[:], x_sb[:, bass.ds(b * NB, NB), :]
                link(TT(y, r1[bp][:, :, 0:F], r2[bp][:, :, 0:F], ALU.add))
                link(TT(y, y, spread(cols(dmask, b), F), ALU.mult))
                TT(y, y, spread(cols(rdeg, b), F), ALU.mult).then_inc(n_v["2"], 1)
                v.wait_ge(n_m["2"], b * 2 + 2)
                o = bank[0][:, 0:NB * (F + 3)].rearrange("p (c f) -> p c f", c=NB)
                g = zb[:, :, 0:3]
                link(TT(g, o[:, :, F:F + 3], spread_mid(bgc[:], NB), ALU.add))
                link(TS(g, g, 0.0, None, ALU.max))
                link(v.tensor_reduce(sm[:, 4, :], g, AX, ALU.max))
                link(TT(g, g, spread(sm[:, 4, :], 3), ALU.is_equal))
                link(v.tensor_reduce(sm[:, 5, :], g, AX, ALU.add))
                link(TT(z, o[:, :, 0:F], spread(sm[:, 5, :], F), ALU.mult))
                link(TT(z, z, spread_mid(blin[:], NB), ALU.add))
                link(TT(z, z, xs, ALU.add))
                norm("2", link, z, b * 3 + 3, xs).then_inc(n_use["2"], 1)
                v.wait_ge(n_use["2"], b + 1)

            carry(1, F, 1, c_s)
            batches("2", 15, stage2)

            def mask_x3(n, i):
                TT(xm[i][:], spread_mid(x_sb[:, bass.ds(n, 1), :].rearrange("p a f -> p (a f)"), NTY),
                   spread(nmask[:, :, bass.ds(n, 1)].rearrange("p y a -> p (y a)"), F), ALU.mult).then_inc(tv, 1)

            mask_x3(0, 0)
            with loop(v, 0, NT - 1, 2) as n:
                for i in range(2):
                    v.wait_ge(tp1, n + (i + 1))
                    mask_x3(n + (i + 1), 1 - i)
                    v.wait_ge(tp2, n + (i + 1))
                    v.tensor_copy(side[:, bass.ds(n + i, 1), :].rearrange("p a f -> p (a f)"),
                                  pair[0][:, 512:512 + F]).then_inc(tq, 1)

            def rows3(tp):
                return run_sb[tp][:].rearrange("p s (k h d) -> p s k h d", k=KS, h=H)

            zrow = zst[:].rearrange("p s (h d) -> p s h d", h=H)

            def before3(tp, k, first):
                if k:
                    return rows3(tp)[:, :, k - 1]
                return zrow if first else rows3(1 - tp)[:, :, KS - 1]

            def weigh(t, tp, k):
                n, q = t * KS + k, (tp + k) % 2
                v.wait_ge(d_ex, n * 2 + 2)
                TT(wm[q][:, :, :, 0:HD], gat[:, k, :, F:2 * F].rearrange("p s (h d) -> p s h d", h=H),
                   spread(wm[q][:, :, :, HD], HD), ALU.mult).then_inc(d_wm, 1)

            def decay(t, tp, k, first):
                n, q = t * KS + k, (tp + k) % 2
                if not (first and k == 0):
                    v.wait_ge(d_acc, n)
                TT(ta[:], before3(tp, k, first)[:, :, :, 0:HR], spread(al[q][:], HR), ALU.mult).then_inc(d_ta, 1)

            def accumulate(t, tp, k):
                n, q = t * KS + k, (tp + k) % 2
                v.wait_ge(d_ta, n + 1)
                v.wait_ge(d_wm, n + 1)
                TT(rows3(tp)[:, :, k, :, 0:HR], ta[:], wm[q][:], ALU.add).then_inc(d_acc, 1)

            def phase_d(t, tp, first):
                v.wait_ge(d_st, t * 3 + 3)
                v.wait_ge(e_in["d"][tp], sides(t, tp))
                v.wait_ge(r_out["d"][tp], sides(t, tp))
                for k in range(KS):
                    n, q = t * KS + k, (tp + k) % 2
                    back = (t, tp, k - 1) if k else None if first else (t - 1, 1 - tp, KS - 1)
                    if not (first and k == 0):
                        v.wait_ge(d_q, n)
                    TT(t1[:], cur[:], spread(ct[tp][:, :, k], F), ALU.mult).then_inc(d_t1, 1)
                    if back:
                        weigh(*back)
                    v.wait_ge(d_t1, n + 1)
                    if not (first and k == 0):
                        v.wait_ge(d_pr, n)
                        v.wait_ge(d_ar, n)
                    TT(cur[:], t1[:], edge0[tp][:, :, k, :], ALU.add).then_inc(d_q, 1)
                    if back:
                        decay(*back, first and k == 1)
                    v.wait_ge(d_q, n + 1)
                    v.wait_ge(g_in["d"][k], t * (16 * SUB) + 16 * SUB)
                    TT(pr[:], gat[:, k, :, 0:F], cur[:], ALU.mult).then_inc(d_pr, 1)
                    if back:
                        accumulate(*back)
                    v.wait_ge(d_pr, n + 1)
                    if not (first and k == 0):
                        v.wait_ge(d_dm, n * 2)
                    v.tensor_reduce(ar[:], pr[:].rearrange("p s (h d) -> p s h d", h=H), AX, ALU.add
                                    ).then_inc(d_ar, 1)
                    TT(mp[:], before3(tp, k, first)[:, :, :, HR], spread(pn[tp][:, :, k], H), ALU.add
                       ).then_inc(d_mp, 1)
                    v.wait_ge(d_ar, n + 1)
                    v.wait_ge(d_mp, n + 1)
                    mx = rows3(tp)[:, :, k, :, HR]
                    TT(mx, mp[:], ar[:], ALU.max).then_inc(d_m, 1)
                    v.wait_ge(d_m, n + 1)
                    if not (first and k < 2):
                        v.wait_ge(d_ex, n * 2 - 2)
                    TT(dm[q][:, 0], mp[:], mx, ALU.subtract).then_inc(d_dm, 1)
                    TT(dm[q][:, 1], ar[:], mx, ALU.subtract).then_inc(d_dm, 1)
            each_iteration(v, phase_d)
            weigh(T - 1, 0, KS - 1)
            decay(T - 1, 0, KS - 1, False)
            accumulate(T - 1, 0, KS - 1)

            def stage3(b, bp, link):
                y, z, xs = yb[:], zb[:], x_sb[:, bass.ds(b * NB, NB), :]
                a = r1[bp][:].rearrange("p c (h d) -> p c h d", h=H)
                c = r2[bp][:].rearrange("p c (h d) -> p c h d", h=H)
                link(TT(s4[:, 0], a[:, :, :, HR], c[:, :, :, HR], ALU.max))
                link(TT(s4[:, 1], a[:, :, :, HR], s4[:, 0], ALU.subtract))
                TT(s4[:, 2], c[:, :, :, HR], s4[:, 0], ALU.subtract).then_inc(n_v["3"], 1)
                v.wait_ge(n_a2["3"], b * 4 + 1)
                link(TT(a[:, :, :, 0:HR], a[:, :, :, 0:HR], spread(s4[:, 3], HR), ALU.mult))
                link(TT(c[:, :, :, 0:HR], c[:, :, :, 0:HR], spread(s4[:, 4], HR), ALU.mult))
                link(TT(a[:, :, :, 0:HR], a[:, :, :, 0:HR], c[:, :, :, 0:HR], ALU.add))
                link(v.reciprocal(s4[:, 5], a[:, :, :, HD]))
                link(TT(s4[:, 5], s4[:, 5], spread(cols(dmask, b), H), ALU.mult))
                TT(y.rearrange("p c (h d) -> p c h d", h=H), a[:, :, :, 0:HD], spread(s4[:, 5], HD), ALU.mult
                   ).then_inc(n_v["3"], 1)
                v.wait_ge(n_m["3"], b * 2 + 2)
                for c0, n, o in ((0, 4, pair[1]), (4, NB - 4, pair[0])):
                    for ty in range(NTY):
                        prod = o[:, 0:n * 256].rearrange("p (c a f) -> p c a f", c=n, a=NTY)[:, :, ty, :]
                        m = spread(nmask[:, ty, bass.ds(b * NB + c0, n)], F)
                        zz = z[:, c0:c0 + n, :]
                        if ty == 0:
                            link(TT(zz, prod, m, ALU.mult))
                        else:
                            link(TT(sel[:, c0:c0 + n, :], prod, m, ALU.mult))
                            link(TT(zz, zz, sel[:, c0:c0 + n, :], ALU.add))
                link(TT(z, z, xs, ALU.add))
                norm("3", link, z, b * 4 + 4, xs).then_inc(n_use["3"], 1)
                v.wait_ge(n_use["3"], b + 1)

            carry(2, H * HR, 2, d_acc)
            batches("3", 27, stage3)


_INS = ["x", "src", "dst", "edge_attr_64", "edge_type_8", "node_type_4"]
_WEIGHTS = ["L0_gnn_W1", "L0_gnn_b1", "L0_gnn_W2", "L0_gnn_b2", "L1_gnn_u", "L1_gnn_W1", "L1_gnn_b1",
            "L1_gnn_W2", "L1_gnn_b2", "L2_gnn_W_gc", "L2_gnn_b_gc", "L2_gnn_b_lin", "L3_gnn_Wk", "L3_gnn_Wq",
            "L3_gnn_Wv", "L3_gnn_Wa", "L3_gnn_rel_msg", "L3_gnn_rel_pri"]


def kernel(**inputs):
    import numpy as _np
    import concourse.bacc as _bacc
    from concourse import mybir as _mybir
    from concourse.bass_utils import run_bass_kernel_spmd as _run

    nc = _bacc.Bacc("TRN2", target_bir_lowering=False, num_devices=1)
    laid = {n: _np.ascontiguousarray(inputs[n]) for n in _INS + _WEIGHTS}
    laid["L2_W_lin_T"] = _np.ascontiguousarray(_np.asarray(inputs["L2_gnn_W_lin"]).T)
    laid["L3_rel_att_T"] = _np.ascontiguousarray(_np.asarray(inputs["L3_gnn_rel_att"]).transpose(0, 3, 1, 2))
    arrays, aps = {}, {}
    for name, a in laid.items():
        arrays[f"in_{name}"] = a
        aps[name] = nc.dram_tensor(f"in_{name}", a.shape, _mybir.dt.from_np(a.dtype), kind="ExternalInput").ap()
    shape = laid["x"].shape
    out = nc.dram_tensor("out_0", shape, _mybir.dt.float32, kind="ExternalOutput").ap()
    gnn_program(nc, *[aps.pop(n) for n in _INS], aps, out)
    r = _run(nc, [arrays], core_ids=[0])
    return r.results[0]["out_0"]
```
